# Optimizing a Trainium2 kernel written in Bass

```python
import numpy as np
import jax
import jax.numpy as jnp

def _softmax(x, axis=-1):
    return jax.nn.softmax(x, axis=axis)

def _gelu(x):
    return jax.nn.gelu(x, approximate=True)

def _silu(x):
    return jax.nn.silu(x)

def _sigmoid(x):
    return jax.nn.sigmoid(x)

def _layernorm(x, axis=-1, eps=1e-05):
    m = jnp.mean(x, axis=axis, keepdims=True)
    v = jnp.var(x, axis=axis, keepdims=True)
    return (x - m) / jnp.sqrt(v + eps)

def _scatter_add(tgt, idx, src, axis=0):
    return tgt.at[idx].add(src)

def _segment_sum(src, seg, n):
    return jax.ops.segment_sum(src, seg, n)
kernel_name = 'mk_flamingo_gated_d1_seqx_r8_8b3bd0'

def setup_inputs(seed: int=0):
    np.random.seed(seed)
    _w = jnp.asarray

    def _rec_inputs():
        import jax
        import jax.numpy as jnp
        _rk = jax.random.key(seed)
        x = 7.22e-05 + 1 * jax.random.normal(jax.random.fold_in(_rk, 1), (2, 256, 256), jnp.float32)
        _lenS = 256 - jax.random.randint(jax.random.fold_in(_rk, 7), (2,), 0, max(1, 256 // 4) + 1, jnp.int32)
        _lenS2 = 512 - jax.random.randint(jax.random.fold_in(_rk, 8), (2,), 0, max(1, 512 // 4) + 1, jnp.int32)
        _ctx_512P = jax.random.normal(jax.random.fold_in(_rk, 11), (2, 16, 64), jnp.float32)
        _ctx_512c = jax.random.dirichlet(jax.random.fold_in(_rk, 511), 0.3 * jnp.ones((16,), jnp.float32), (2, 512))
        _ctx_512t = jnp.einsum('bsk,bkd->bsd', _ctx_512c, _ctx_512P)
        _ctx_512t = _ctx_512t * jax.lax.rsqrt(jnp.mean(jnp.square(_ctx_512t)) + 1e-12) * 0.953939
        ctx_512 = -0.000514642 + 1.00011 * (_ctx_512t + 0.3 * jax.random.normal(jax.random.fold_in(_rk, 611), (2, 512, 64), jnp.float32))
        _g = jax.random.normal(jax.random.fold_in(_rk, 9001), (2, 1), jnp.float32)
        _g = jnp.sign(_g) * jnp.maximum(jnp.abs(_g), 1.0) + (_g == 0) * 1.0
        g_xattn = _g[0]
        g_ffn = _g[1]
        return (x, ctx_512, g_xattn, g_ffn)
    x, ctx_512, g_xattn, g_ffn = _rec_inputs()

    def _L0_xattn_setup():
        import jax, jax.numpy as jnp
        import numpy as np
        B, S, H, NH, L = (2, 256, 256, 16, 64)
        HD = H // NH
        key = jax.random.key(seed)
        k1, k2, k3, k4, k5 = jax.random.split(key, 5)
        scale = 0.02
        return {'q': jax.random.normal(k1, (B, S, H), dtype=jnp.float32), 'latent_kv': jax.random.normal(k2, (B, S, L), dtype=jnp.float32), 'Wq': jax.random.normal(k3, (H, H), dtype=jnp.float32) * scale, 'Wkv_expand': jax.random.normal(k4, (2 * H, L), dtype=jnp.float32) * scale, 'Wout': jax.random.normal(k5, (H, H), dtype=jnp.float32) * scale}
    _L0_xattn_all = _L0_xattn_setup()
    _L0_xattn_in = {k: v for k, v in _L0_xattn_all.items() if k in ('Wq', 'Wkv_expand', 'Wout')}
    del _L0_xattn_all

    def _L0_ffn_setup():
        import jax, jax.numpy as jnp
        import numpy as np
        TOP_K = 8
        CAPACITY = 128
        key = jax.random.key(seed)
        k1, k2, k3, k4 = jax.random.split(key, 4)
        B, S, H, E, I = (2, 128, 256, 64, 96)
        hidden_states = jax.random.normal(k1, (B, S, H), dtype=jnp.float32)
        router_weight = jax.random.normal(k2, (E, H), dtype=jnp.float32) * 0.02
        gate_up_proj = jax.random.normal(k3, (E, H, 2 * I), dtype=jnp.float32) * 0.02
        down_proj = jax.random.normal(k4, (E, I, H), dtype=jnp.float32) * 0.02
        return {'hidden_states': hidden_states, 'router_weight': router_weight, 'gate_up_proj': gate_up_proj, 'down_proj': down_proj}
    _L0_ffn_all = _L0_ffn_setup()
    _L0_ffn_in = {k: v for k, v in _L0_ffn_all.items() if k in ('router_weight', 'gate_up_proj', 'down_proj')}
    del _L0_ffn_all
    return {'x': x, 'ctx_512': ctx_512, 'g_xattn': g_xattn, 'g_ffn': g_ffn, 'L0_xattn_Wq': _L0_xattn_in['Wq'], 'L0_xattn_Wkv_expand': _L0_xattn_in['Wkv_expand'], 'L0_xattn_Wout': _L0_xattn_in['Wout'], 'L0_ffn_router_weight': _L0_ffn_in['router_weight'], 'L0_ffn_gate_up_proj': _L0_ffn_in['gate_up_proj'], 'L0_ffn_down_proj': _L0_ffn_in['down_proj']}

def reference(x, ctx_512, g_xattn, g_ffn, L0_xattn_Wq, L0_xattn_Wkv_expand, L0_xattn_Wout, L0_ffn_router_weight, L0_ffn_gate_up_proj, L0_ffn_down_proj):
    import jax
    import jax.numpy as jnp

    def _L0_xattn_ref(q, latent_kv, Wq, Wkv_expand, Wout):
        import jax, jax.numpy as jnp
        import numpy as np
        B, S, H, NH, L = (2, 256, 256, 16, 64)
        HD = H // NH
        b, sq, _ = q.shape
        sk = latent_kv.shape[1]
        qp = q @ Wq.T
        kv = latent_kv @ Wkv_expand.T
        k, v = jnp.split(kv, 2, axis=-1)
        qh = qp.reshape(b, sq, NH, HD).transpose(0, 2, 1, 3)
        kh = k.reshape(b, sk, NH, HD).transpose(0, 2, 1, 3)
        vh = v.reshape(b, sk, NH, HD).transpose(0, 2, 1, 3)
        inv_sqrt_d = 1.0 / jnp.sqrt(jnp.float32(HD))
        scores = jnp.einsum('bhqd,bhkd->bhqk', qh, kh) * inv_sqrt_d
        causal = jnp.tril(jnp.ones((sq, sk), dtype=bool))
        scores = jnp.where(causal, scores, jnp.finfo(scores.dtype).min)
        attn = jax.nn.softmax(scores, axis=-1)
        out = jnp.einsum('bhqk,bhkd->bhqd', attn, vh)
        out = out.transpose(0, 2, 1, 3).reshape(b, sq, H)
        return out @ Wout.T

    def _L0_ffn_ref(hidden_states, router_weight, gate_up_proj, down_proj):
        import jax, jax.numpy as jnp
        import numpy as np
        TOP_K = 8
        CAPACITY = 128
        B, S, H = hidden_states.shape
        E = router_weight.shape[0]
        K, C = (TOP_K, CAPACITY)
        x = hidden_states.reshape(-1, H)
        logits = x @ router_weight.T
        probs = jax.nn.softmax(logits, axis=-1)
        topw, topi = jax.lax.top_k(probs, K)
        topw = topw / jnp.sum(topw, axis=-1, keepdims=True)
        flat_e = topi.reshape(-1)
        oh = jax.nn.one_hot(flat_e, E, dtype=jnp.int32)
        pos = jnp.take_along_axis(jnp.cumsum(oh, axis=0), flat_e[:, None], axis=1)[:, 0] - 1
        x_rep = jnp.repeat(x, K, axis=0)
        xe = jnp.zeros((E, C, H), x.dtype).at[flat_e, pos].set(x_rep, mode='drop')
        gu = jnp.einsum('ech,ehf->ecf', xe, gate_up_proj)
        g, u = jnp.split(gu, 2, axis=-1)
        h = jax.nn.silu(g) * u
        ye = jnp.einsum('eci,eih->ech', h, down_proj)
        valid = pos < C
        y_flat = jnp.where(valid[:, None], ye[flat_e, jnp.minimum(pos, C - 1)], 0.0)
        y = jnp.sum(y_flat.reshape(-1, K, H) * topw.reshape(-1, K)[..., None], axis=1)
        return y.reshape(B, S, H)
    x = x + jnp.tanh(g_xattn[0]) * _L0_xattn_ref(_layernorm(x, axis=-1), ctx_512, L0_xattn_Wq, L0_xattn_Wkv_expand, L0_xattn_Wout)
    x = x + jnp.tanh(g_ffn[0]) * _L0_ffn_ref(_layernorm(x, axis=-1), L0_ffn_router_weight, L0_ffn_gate_up_proj, L0_ffn_down_proj)
    return x

_drawn_inputs = setup_inputs


def setup_inputs(seed=0):
    import zlib

    import numpy as np

    out = dict(_drawn_inputs(seed))
    spreads = {}
    factors = {'L0_xattn_Wq': 8.0,
     'L0_xattn_Wkv_expand': 2.689,
     'L0_xattn_Wout': 2.8,
     'L0_ffn_router_weight': 8.0,
     'L0_ffn_gate_up_proj': 8.0,
     'L0_ffn_down_proj': 8.0}
    for name, (base, spread) in spreads.items():
        noise = np.random.default_rng([zlib.crc32(name.encode()), seed]).standard_normal(out[name].shape)
        drawn = base * np.exp(spread * noise) if base else spread * noise
        out[name] = jnp.asarray(drawn.astype(out[name].dtype))
    for name, factor in factors.items():
        out[name] = (out[name] * factor).astype(out[name].dtype)
    return out
```

```python
from contextlib import ExitStack

import concourse.bass as bass
from concourse import mybir

ALU = mybir.AluOpType
ACT = mybir.ActivationFunctionType
AX = mybir.AxisListType
F32 = mybir.dt.float32
BF16 = mybir.dt.bfloat16
U32 = mybir.dt.uint32

P = 128
B, S, H = 2, 256, 256
NH, HD, L = 16, 16, 64
E, I, TOPK, CAP = 64, 96, 8, 128
TILES = B * S // P
QT = S // P
KC = H // P
VW = HD + 1
HP = 32
HEADS = B * NH
EPS = 1e-5
BIG = 1e30
NO_TOKEN = 1024
XE_RING = Y_RING = 4
UNROLL = 8
LOOKAHEAD = 8
EARLY = 48
CHUNK = 4
C_RING = 8


class Expert:

    def __init__(self, i, u):
        self.i, self.slot = i + u // UNROLL, u % UNROLL
        self.e = self.i * UNROLL + self.slot
        self.static = isinstance(self.i, int)

    def plus(self, d):
        return Expert(self.i, self.slot + d)

    def from_(self, first):
        return not self.static or self.e >= first

    def exists(self):
        return not self.static or 0 <= self.e < E


def pipeline(eng, step):
    for s in range(-LOOKAHEAD, UNROLL):
        step(Expert(0, s))
    with eng.Fori(1, (E - LOOKAHEAD) // UNROLL) as i:
        for u in range(UNROLL):
            step(Expert(i, u))
    for s in range(E - LOOKAHEAD, E + 2):
        step(Expert(0, s))


def flamingo_moe(nc, x, ctx_kv, g_xattn, g_ffn, wq, wkv, wout, router, gate_up, down, out):
    with ExitStack() as stack:
        def sb(name, shape, dt=F32):
            return stack.enter_context(nc.sbuf_tensor(name, shape, dt))

        def sem(name):
            return stack.enter_context(nc.semaphore(name))

        bank = [stack.enter_context(nc.psum_tensor(f"bank{i}", [P, 512], F32)) for i in range(8)]
        xn2_dram = nc.dram_tensor("xn2_dram", (TILES * P, H), F32, kind="Internal").ap()
        ye_dram = nc.dram_tensor("ye_dram", (E * CAP, H), F32, kind="Internal").ap()

        gate_w = sb("gate_w", [P, E, KC * 2 * I])
        down_w = sb("down_w", [I, E, H])
        x_sb = sb("x_sb", [P, TILES, H])
        xn = sb("xn", [P, TILES, H])
        ident = sb("ident", [P, P])
        mask = sb("mask", [P, 3 * P])
        slot1 = sb("slot1", [P, P], BF16)
        earlier = sb("earlier", [P, P], BF16)
        ones = sb("ones", [P, P], BF16)
        token_id = sb("token_id", [P, TILES, 2], BF16)
        gates = sb("gates", [P, 2])
        tgates = sb("tgates", [P, 2])
        eps = sb("eps", [P, 1])
        stats = sb("stats", [P, TILES, 6])
        mv = sb("mv", [P, TILES, 2])
        std = sb("std", [P, TILES])
        rstd = sb("rstd", [P, TILES])
        rmin = sb("rmin", [P, HEADS, QT])
        place1 = sb("place1", [P, TILES, E])
        slot_token = sb("slot_token", [P, UNROLL], U32)
        row8 = sb("row8", [P, TILES, TOPK], U32)
        w8 = sb("w8", [P, TILES, TOPK])
        wout_sb = sb("wout_sb", [P, KC, H])
        router_sb = sb("router_sb", [E, H])
        woT = sb("woT", [P, KC, H])
        rT = sb("rT", [P, KC, E])
        expert_row1 = sb("expert_row1", [P, E])
        work = sb("work", [P, 6016])

        def carver(tensor, words):
            used = [0]

            def take(n, dt=F32, parts=P):
                a = tensor[0:parts, used[0]:used[0] + n]
                used[0] += n
                assert used[0] <= words
                return a if dt == F32 else a.bitcast(dt)
            return take

        take = carver(gate_w[:, EARLY:E, :].rearrange("p e n -> p (e n)"), (E - EARLY) * KC * 2 * I)
        qT = take(4 * B * S).rearrange("p (g t) -> p g t", g=4)
        kT = take(4 * B * S).rearrange("p (g t) -> p g t", g=4)
        v_sb = take(TILES * NH * VW).rearrange("p (t h w) -> p t h w", t=TILES, w=VW)
        take = carver(work, 6016)
        wq_sb = take(KC * H).rearrange("p (o i) -> p o i", o=KC)
        wkv_sb = take(4 * L).rearrange("p (r l) -> p r l", r=4)
        ctx_sb = take(TILES * L).rearrange("p (t l) -> p t l", t=TILES)
        xnT = take(KC * B * S).rearrange("p (k t) -> p k t", k=KC)
        wqT = take(KC * NH * HP).rearrange("p (k h d) -> p k h d", k=KC, d=HP)
        wkT = take(NH * HP, parts=L).rearrange("p (h d) -> p h d", d=HP)
        wvT = take(H, parts=L)
        ctxT = take(B * S, parts=L)
        take = carver(work, 6016)
        score = [take(3 * P) for _ in range(3)]
        probT = [take(3 * P) for _ in range(2)]
        att = take(TILES * H).rearrange("p (t n) -> p t n", t=TILES)
        attT = [take(KC * P).rearrange("p (k t) -> p k t", k=KC) for _ in range(2)]
        xn2T = [take(KC * P).rearrange("p (k t) -> p k t", k=KC) for _ in range(2)]
        o_rden = take(QT * NH)
        rp = take(TILES * E).rearrange("p (t e) -> p t e", t=TILES)
        rp2 = take(TILES * E).rearrange("p (t e) -> p t e", t=TILES)
        rsel = take(TILES * E).rearrange("p (t e) -> p t e", t=TILES)
        rselb = take(TILES * E // 2, BF16).rearrange("p (t e) -> p t e", t=TILES)
        top = take(TILES * TOPK).rearrange("p (t k) -> p t k", t=TILES)
        rstat = take(4 * TILES).rearrange("p (n t) -> p n t", n=4)
        keep = take(TILES * E).rearrange("p (t e) -> p t e", t=TILES)
        row1 = take(TILES * E).rearrange("p (t e) -> p t e", t=TILES)
        row8f = take(TILES * TOPK).rearrange("p (t k) -> p t k", t=TILES)
        match = take(TOPK * E).rearrange("p (k e) -> p k e", k=TOPK)
        take = carver(work, 6016)
        onehot = [take(TILES * P // 2, BF16).rearrange("p (t s) -> p t s", t=TILES) for _ in range(2)]
        y_sb = [take(H) for _ in range(Y_RING)]
        xeT = [take(KC * P).rearrange("p (k t) -> p k t", k=KC) for _ in range(2)]
        sil = [take(I) for _ in range(2)]
        hid = [take(I) for _ in range(2)]
        hT = [take(P, parts=I) for _ in range(2)]
        xe = sb("xe", [P, XE_RING, H])
        c_sb = gate_w[:, 0:6, :].rearrange("p e n -> p (e n)")[:, 0:C_RING * H].rearrange("p (r n) -> p r n", r=C_RING)
        acc = gate_w[:, 6:9, :].rearrange("p e n -> p (e n)")[:, 0:TILES * H].rearrange("p (t n) -> p t n", t=TILES)

        x_in, wq_in, ctx_in, wkv_in, wout_in, router_in, gates_in = (
            sem(n) for n in ("x_in", "wq_in", "ctx_in", "wkv_in", "wout_in", "router_in", "gates_in"))
        gate_w_in, gate_w_late_in, down_w_in = sem("gate_w_in"), sem("gate_w_late_in"), sem("down_w_in")
        consts = sem("consts")
        turned = sem("turned")
        wqT_done, wkvT_done, ctxT_done, woT_done, rT_done = (
            sem(n) for n in ("wqT_done", "wkvT_done", "ctxT_done", "woT_done", "rT_done"))
        xn_done, xnT_done = sem("xn_done"), sem("xnT_done")
        std_done, var_done = sem("std_done"), sem("var_done")
        k_mm, k_done, v_mm, v_done, q_mm, q_done = (
            sem(n) for n in ("k_mm", "k_done", "v_mm", "v_done", "q_mm", "q_done"))
        scored, masked, exped, probs_turned = (sem(n) for n in ("scored", "masked", "exped", "probs_turned"))
        probT_act, probT_dve, pv_done, att_done = (sem(n) for n in ("probT_act", "probT_dve", "pv_done", "att_done"))
        att_turned, attT_done, projected, x1_done = (sem(n) for n in ("att_turned", "attT_done", "projected", "x1_done"))
        tanh_done, xn2_done, xn2_stored = sem("tanh_done"), sem("xn2_done"), sem("xn2_stored")
        xn2_turned, xn2T_done, logits_done = sem("xn2_turned"), sem("xn2T_done"), sem("logits_done")
        shifted, routed, selected, counted, placed = (
            sem(n) for n in ("shifted", "routed", "selected", "counted", "placed"))
        onehot_done, slots_mm, slots_done, rows_ready = (
            sem(n) for n in ("onehot_done", "slots_mm", "slots_done", "rows_ready"))
        xe_cleared = sem("xe_cleared")
        xe_in = [sem(f"xe_in{i}") for i in range(UNROLL)]
        xe_turned, xeT_done, gu_mm, silu_done, hid_done, hid_turned, hT_done, y_mm, y_done = (
            sem(n) for n in ("xe_turned", "xeT_done", "gu_mm", "silu_done", "hid_done", "hid_turned",
                             "hT_done", "y_mm", "y_done"))
        y_out = [sem(f"y_out{i}") for i in range(UNROLL)]
        c_in = [sem(f"c_in{i}") for i in range(C_RING)]
        combined, out_done, stored = sem("combined"), sem("out_done"), sem("stored")
        dve_step, act_step = sem("dve_step"), sem("act_step")
        N_CONSTS = 17

        x_tiles = x.rearrange("b (t p) h -> p (b t) h", p=P)
        out_tiles = out.rearrange("b (t p) h -> p (b t) h", p=P)
        block = stack.enter_context(nc.Block())

        @block.sync
        def _(sp):
            sp.dma_start(x_sb[:], x_tiles).then_inc(x_in, 16)
            sp.dma_start(wkv_sb, wkv.rearrange("(r p) l -> p r l", p=P)).then_inc(wkv_in, 16)
            for b in range(B):
                sp.dma_start(ctx_sb[:, QT * b:QT * b + QT, :],
                             ctx_kv[b, 0:S, :].rearrange("(t p) l -> p t l", p=P)).then_inc(ctx_in, 16)
            sp.dma_start(wq_sb, wq.rearrange("(o p) i -> p o i", p=P)).then_inc(wq_in, 16)
            sp.dma_start(gates[:, 0:1], g_xattn.partition_broadcast(P)).then_inc(gates_in, 16)
            sp.dma_start(gates[:, 1:2], g_ffn.partition_broadcast(P)).then_inc(gates_in, 16)
            sp.dma_start(wout_sb[:], wout.rearrange("(o p) i -> p o i", p=P)).then_inc(wout_in, 16)
            sp.dma_start(router_sb[:], router).then_inc(router_in, 16)

            def load_gate(e, signal):
                sp.dma_start(gate_w[:, e:e + CHUNK, :],
                             gate_up[e:e + CHUNK].rearrange("e (p c) f -> p e (c f)", c=KC)).then_inc(signal, 16)

            for e in range(0, E, CHUNK):
                if e < EARLY:
                    load_gate(e, gate_w_in)
                sp.dma_start(down_w[:, e:e + CHUNK, :],
                             down[e:e + CHUNK].rearrange("e i h -> i e h")).then_inc(down_w_in, 16)
            for t in range(TILES):
                if t == 0:
                    sp.wait_ge(pv_done, HEADS)
                    for e in range(EARLY, E, CHUNK):
                        load_gate(e, gate_w_late_in)
                sp.wait_ge(xn2_done, t + 1)
                sp.dma_start(xn2_dram[t * P:t * P + P, :], xn[:, t, :]).then_inc(xn2_stored, 16)

            def store_y(e):
                sp.wait_ge(y_done, e.e + 1)
                sp.dma_start(ye_dram.rearrange("(e s) h -> s e h", s=CAP)[:, bass.ds(e.e, 1), :]
                             .rearrange("s a h -> s (a h)"), y_sb[e.slot % Y_RING]).then_inc(y_out[e.slot], 16)

            with sp.Fori(0, E // UNROLL) as i:
                for u in range(UNROLL):
                    store_y(Expert(i, u))
            for t in range(TILES):
                sp.wait_ge(out_done, t + 1)
                sp.dma_start(out_tiles[:, t, :], xn[:, t, :]).then_inc(stored, 16)
            sp.wait_ge(stored, 16 * TILES)

        @block.gpsimd
        def _(pool):
            pool.memset(ident[:], 0.0).then_inc(consts, 1)
            pool.wait_ge(consts, 1)
            pool.affine_select(out=ident[:], in_=ident[:], compare_op=ALU.not_equal, fill=1.0, base=0,
                               pattern=[[-1, P]], channel_multiplier=1).then_inc(consts, 1)
            pool.memset(wqT[:, :, :, HD:HP], 0.0).then_inc(consts, 1)
            pool.memset(wkT[:, :, HD:HP], 0.0).then_inc(consts, 1)
            pool.memset(v_sb[:, :, :, HD:VW], 1.0).then_inc(consts, 1)
            pool.memset(eps[:], EPS).then_inc(consts, 1)
            pool.memset(mask[:], 0.0).then_inc(consts, 1)
            pool.wait_ge(consts, 7)
            for c in (0, 2):
                pool.affine_select(out=mask[:, c * P:c * P + P], in_=mask[:, c * P:c * P + P],
                                   compare_op=ALU.is_ge, fill=BIG, base=0, pattern=[[-1, P]],
                                   channel_multiplier=1).then_inc(consts, 1)
            pool.memset(ones[:], 1.0).then_inc(consts, 1)
            pool.wait_ge(consts, 10)
            pool.affine_select(out=earlier[:], in_=ones[:], compare_op=ALU.is_gt, fill=0.0, base=0,
                               pattern=[[1, P]], channel_multiplier=-1).then_inc(consts, 1)
            pool.iota(slot1[:], pattern=[[1, P]], base=1, channel_multiplier=0,
                      allow_small_or_imprecise_dtypes=True).then_inc(consts, 1)
            pool.iota(token_id[:, :, 0], pattern=[[0, TILES]], base=0, channel_multiplier=1,
                      allow_small_or_imprecise_dtypes=True).then_inc(consts, 1)
            pool.iota(token_id[:, :, 1], pattern=[[P, TILES]], base=-NO_TOKEN, channel_multiplier=0,
                      allow_small_or_imprecise_dtypes=True).then_inc(consts, 1)
            pool.iota(expert_row1[:], pattern=[[CAP, E]], base=1, channel_multiplier=0,
                      allow_small_or_imprecise_dtypes=True).then_inc(consts, 1)
            pool.memset(xe[:], 0.0).then_inc(consts, 1)
            pool.memset(rmin[:], 0.0).then_inc(consts, 1)
            pool.wait_ge(consts, N_CONSTS)

            pool.wait_ge(xn2_stored, 16 * TILES)

            last_token = pool.to_reg(TILES * P - 1)

            def gather(e):
                pool.wait_ge(slots_done, e.e + 1)
                if e.from_(XE_RING):
                    pool.wait_ge(xe_turned, e.e - XE_RING + 1)
                pool.indirect_dma_start(
                    out=xe[:, e.slot % XE_RING, :], out_offset=None, in_=xn2_dram,
                    in_offset=bass.IndirectOffsetOnAxis(ap=slot_token[:, e.slot:e.slot + 1], axis=0),
                    bounds_check=last_token, oob_is_err=False).then_inc(xe_in[e.slot], 16)

            for e in range(E):
                gather(Expert(0, e))

            for u in range(UNROLL):
                pool.wait_ge(y_out[u], 16 * (E // UNROLL))
            pool.wait_ge(rows_ready, TILES)
            pool.wait_ge(gu_mm, E)

            def gather_rows(t, first):
                for k in range(TOPK):
                    if not first:
                        pool.wait_ge(combined, t * TOPK + (k + 1 - TOPK))
                    pool.indirect_dma_start(
                        out=c_sb[:, k, :], out_offset=None, in_=ye_dram,
                        in_offset=bass.IndirectOffsetOnAxis(ap=row8[:, t, k:k + 1], axis=0),
                        bounds_check=E * CAP - 1, oob_is_err=False).then_inc(c_in[k], 16)

            for t in range(TILES):
                gather_rows(t, t == 0)

        @block.tensor
        def _(pe):
            def turn_blocks(pairs, signal):
                for src, d in pairs:
                    k, m = src.shape
                    last = nc.tensor.transpose(d, src, ident[0:k, 0:k])
                last.then_inc(signal, 1)

            pe.wait_ge(consts, 2)
            pe.wait_ge(wkv_in, 16)
            turn_blocks([(wkv_sb[:, r, :], bank[1][0:L, r * P:r * P + P]) for r in range(4)], turned)
            pe.wait_ge(ctx_in, 32)
            turn_blocks([(ctx_sb[:, t, :], bank[2][0:L, t * P:t * P + P]) for t in range(TILES)], turned)
            pe.wait_ge(wq_in, 16)
            turn_blocks([(wq_sb[:, o, k * P:k * P + P], bank[0][:, (k * KC + o) * P:(k * KC + o + 1) * P])
                               for k in range(KC) for o in range(KC)], turned)
            pe.wait_ge(wkvT_done, 2)
            pe.wait_ge(ctxT_done, 1)
            pe.wait_ge(consts, N_CONSTS)
            for g in range(4):
                nc.tensor.matmul(bank[4 + g][:], wkT[:, 4 * g:4 * g + 4, :].rearrange("p h d -> p (h d)"), ctxT,
                                 start=True, stop=True).then_inc(k_mm, 1)
            pe.wait_ge(xn_done, TILES)
            for k in range(KC):
                if k == 0:
                    pe.wait_ge(ctxT_done, 1)
                turn_blocks([(xn[:, t, k * P:k * P + P], bank[2 + k][:, t * P:t * P + P])
                                   for t in range(TILES)], turned)
            pe.wait_ge(wqT_done, 1)
            for t in range(TILES):
                last = nc.tensor.matmul(bank[t // 2][:, (t % 2) * H:(t % 2) * H + H], ctxT[:, t * P:t * P + P], wvT,
                                        start=True, stop=True)
                if t % 2:
                    last.then_inc(v_mm, 1)
            pe.wait_ge(xnT_done, KC)
            for g in range(4):
                pe.wait_ge(k_done, g + 1)
                for k in range(KC):
                    last = nc.tensor.matmul(bank[4 + g][:],
                                            wqT[:, k, 4 * g:4 * g + 4, :].rearrange("p h d -> p (h d)"),
                                            xnT[:, k, :], start=(k == 0), stop=(k == KC - 1))
                last.then_inc(q_mm, 1)
            pe.wait_ge(wout_in, 16)
            pe.wait_ge(v_done, 2)
            turn_blocks([(wout_sb[:, o, k * P:k * P + P], bank[0][:, (k * KC + o) * P:(k * KC + o + 1) * P])
                               for k in range(KC) for o in range(KC)], turned)
            pe.wait_ge(router_in, 16)
            turn_blocks([(router_sb[:, k * P:k * P + P], bank[1][:, k * E:k * E + E]) for k in range(KC)], turned)

            pe.wait_ge(woT_done, 1)
            pe.wait_ge(rT_done, 1)
            pe.wait_ge(q_done, 4)

            def scores(n):
                b, h = n // NH, n % NH
                g, j = h // 4, h % 4
                rows = slice(HP * j, HP * j + HP)
                if n >= 4:
                    pe.wait_ge(masked, 2 * (n - 3))
                nc.tensor.matmul(bank[j][:, 0:P], qT[rows, g, b * S:b * S + P], kT[rows, g, b * S:b * S + P],
                                 start=True, stop=True)
                nc.tensor.matmul(bank[j][:, P:3 * P], qT[rows, g, b * S + P:b * S + S], kT[rows, g, b * S:b * S + S],
                                 start=True, stop=True).then_inc(scored, 1)

            def turn_probs(n):
                pe.wait_ge(exped, 2 * n + 2)
                if n >= 2:
                    pe.wait_ge(probT_act if n % 2 == 0 else probT_dve, (n - 2) // 2 + 1)
                for c in range(3):
                    last = nc.tensor.transpose(bank[4 + n % 2][:, c * P:c * P + P], score[n % 3][:, c * P:c * P + P],
                                               ident[:])
                last.then_inc(probs_turned, 1)

            def values(n):
                b, h = n // NH, n % NH
                pe.wait_ge(probT_act if n % 2 == 0 else probT_dve, n // 2 + 1)
                if n == NH:
                    pe.wait_ge(att_done, 1)
                cols = slice(h * VW, h * VW + VW)
                pt = probT[n % 2]
                nc.tensor.matmul(bank[6][:, cols], pt[:, 0:P], v_sb[:, QT * b, h, :], start=True, stop=True)
                nc.tensor.matmul(bank[7][:, cols], pt[:, P:2 * P], v_sb[:, QT * b, h, :], start=True, stop=False)
                nc.tensor.matmul(bank[7][:, cols], pt[:, 2 * P:3 * P], v_sb[:, QT * b + 1, h, :],
                                 start=False, stop=True).then_inc(pv_done, 1)

            for i in range(HEADS + 3):
                if i < HEADS:
                    scores(i)
                if 0 <= i - 2 < HEADS:
                    turn_probs(i - 2)
                if i >= 3:
                    values(i - 3)

            pe.wait_ge(masked, 2 * HEADS)
            for t in range(TILES):
                pe.wait_ge(att_done, t // 2 + 1)
                turn_blocks([(att[:, t, k * P:k * P + P], bank[t][:, k * P:k * P + P]) for k in range(KC)],
                            att_turned)
            pe.wait_ge(probT_act, HEADS // 2)
            pe.wait_ge(probT_dve, HEADS // 2)
            for t in range(TILES):
                pe.wait_ge(attT_done, t + 1)
                if t >= 2:
                    pe.wait_ge(x1_done, t - 1)
                for k in range(KC):
                    last = nc.tensor.matmul(bank[4 + t % 2][:, 0:H], attT[t % 2][:, k, :], woT[:, k, :],
                                            start=(k == 0), stop=(k == KC - 1))
                last.then_inc(projected, 1)
            for t in range(TILES):
                pe.wait_ge(xn2_done, t + 1)
                if t == 0:
                    pe.wait_ge(attT_done, TILES)
                turn_blocks([(xn[:, t, k * P:k * P + P], bank[t][:, k * P:k * P + P]) for k in range(KC)],
                            xn2_turned)
            pe.wait_ge(att_done, 2)
            for t in range(TILES):
                pe.wait_ge(xn2T_done, t + 1)
                for k in range(KC):
                    last = nc.tensor.matmul(bank[6][:, t * E:t * E + E], xn2T[t % 2][:, k, :], rT[:, k, :],
                                            start=(k == 0), stop=(k == KC - 1))
                last.then_inc(logits_done, 1)
            pe.wait_ge(selected, 1)
            for t in range(TILES):
                for q in range(t + 1):
                    last = nc.tensor.matmul(bank[7][:, t * E:t * E + E], earlier[:] if q == t else ones[:],
                                            rselb[:, q, :], start=(q == 0), stop=(q == t))
            last.then_inc(counted, 1)

            pe.wait_ge(gate_w_in, 16 * (EARLY // CHUNK))
            pe.wait_ge(gate_w_late_in, 16 * ((E - EARLY) // CHUNK))
            pe.wait_ge(down_w_in, 16 * (E // CHUNK))

            def step(s):
                a = s.plus(LOOKAHEAD - 1)
                if a.exists():
                    pe.wait_ge(onehot_done, a.e + 1)
                    if a.from_(1):
                        pe.wait_ge(slots_done, a.e)
                    for t in range(TILES):
                        last = nc.tensor.matmul(bank[0][:, 0:2], onehot[a.slot % 2][:, t, :], token_id[:, t, :],
                                                start=(t == 0), stop=(t == TILES - 1))
                    last.then_inc(slots_mm, 1)
                a = s.plus(1)
                if a.exists():
                    pe.wait_ge(xe_in[a.slot], a.i * 16 + 16)
                    if a.from_(2):
                        pe.wait_ge(xeT_done, a.e - 1)
                    rows = xe[:, a.slot % XE_RING, :].rearrange("s (p c) -> s c p", c=KC)
                    for c in range(KC):
                        last = nc.tensor.transpose(bank[1 + a.slot % 2][:, c * P:c * P + P], rows[:, c, :], ident[:])
                    last.then_inc(xe_turned, 1)
                a = s
                if a.exists():
                    pe.wait_ge(xeT_done, a.e + 1)
                    if a.from_(2):
                        pe.wait_ge(hid_done, a.e - 1)
                    w = gate_w[:, bass.ds(a.e, 1), :].rearrange("p a n -> p (a n)")
                    for c in range(KC):
                        last = nc.tensor.matmul(bank[3 + a.slot % 2][:, 0:2 * I], xeT[a.slot % 2][:, c, :],
                                                w[:, c * 2 * I:(c + 1) * 2 * I], start=(c == 0), stop=(c == KC - 1))
                    last.then_inc(gu_mm, 1)
                a = s.plus(-2)
                if a.exists():
                    pe.wait_ge(hT_done, a.e + 1)
                    if a.from_(2):
                        pe.wait_ge(y_done, a.e - 1)
                    w = down_w[:, bass.ds(a.e, 1), :].rearrange("p a n -> p (a n)")
                    nc.tensor.matmul(bank[6 + a.slot % 2][:, 0:H], hT[a.slot % 2], w,
                                     start=True, stop=True).then_inc(y_mm, 1)
                a = s.plus(-1)
                if a.exists():
                    pe.wait_ge(hid_done, a.e + 1)
                    if a.from_(1):
                        pe.wait_ge(hT_done, a.e)
                    nc.tensor.transpose(bank[5][0:I, 0:P], hid[a.slot % 2], ident[:]).then_inc(hid_turned, 1)

            pipeline(pe, step)

        @block.scalar
        def _(act):
            copy = nc.scalar.copy
            act.wait_ge(turned, 2)
            copy(ctxT, bank[2][0:L, :]).then_inc(ctxT_done, 1)
            act.wait_ge(consts, N_CONSTS)
            act.wait_ge(var_done, 1)
            nc.scalar.activation(std[:], mv[:, :, 1], ACT.Sqrt, bias=eps[:]).then_inc(std_done, 1)
            for g in range(4):
                if g % 2:
                    act.wait_ge(k_mm, g + 1)
                    copy(kT[:, g, :], bank[4 + g][:]).then_inc(act_step, 1)
                    act.wait_ge(act_step, g // 2 + 1)
                    act.wait_ge(k_done, g)
                    nc.scalar.sem_inc(k_done, 1)
            act.wait_ge(turned, 5)
            copy(xnT[:, 1, :], bank[3][:]).then_inc(xnT_done, 1)
            act.wait_ge(v_mm, 2)
            for t in (2, 3):
                last = copy(v_sb[:, t, :, 0:HD], bank[1][:, (t % 2) * H:(t % 2) * H + H]
                            .rearrange("p (h d) -> p h d", d=HD))
            last.then_inc(v_done, 1)
            for g in (1, 3):
                act.wait_ge(q_mm, g + 1)
                copy(qT[:, g, :], bank[4 + g][:]).then_inc(q_done, 1)
            act.wait_ge(turned, 6)
            copy(woT[:].rearrange("p k n -> p (k n)"), bank[0][:]).then_inc(woT_done, 1)
            act.wait_ge(turned, 7)
            copy(rT[:].rearrange("p k n -> p (k n)"), bank[1][:, 0:KC * E]).then_inc(rT_done, 1)
            act.wait_ge(gates_in, 32)
            nc.scalar.activation(tgates[:], gates[:], ACT.Tanh).then_inc(tanh_done, 1)

            for i in range(HEADS + 2):
                if i < HEADS:
                    for qt in range(QT):
                        act.wait_ge(masked, 2 * i + qt + 1)
                        part = score[i % 3][:, 0:P] if qt == 0 else score[i % 3][:, P:3 * P]
                        nc.scalar.activation(part, part, ACT.Exp, bias=rmin[:, i, qt:qt + 1],
                                             scale=-1.0).then_inc(exped, 1)
                n = i - 2
                if 0 <= n < HEADS and n % 2 == 0:
                    act.wait_ge(probs_turned, n + 1)
                    if n >= 2:
                        act.wait_ge(pv_done, n - 1)
                    copy(probT[0], bank[4][:, 0:3 * P]).then_inc(probT_act, 1)
            for t in range(TILES):
                act.wait_ge(att_turned, t + 1)
                if t >= 2:
                    act.wait_ge(projected, t - 1)
                copy(attT[t % 2].rearrange("p k t -> p (k t)"), bank[t][:, 0:KC * P]).then_inc(attT_done, 1)
            for t in range(TILES):
                act.wait_ge(var_done, t + 2)
                nc.scalar.activation(std[:, t:t + 1], mv[:, t, 1:2], ACT.Sqrt, bias=eps[:]).then_inc(std_done, 1)
            for t in range(TILES):
                act.wait_ge(xn2_turned, t + 1)
                if t >= 2:
                    act.wait_ge(logits_done, t - 1)
                copy(xn2T[t % 2].rearrange("p k t -> p (k t)"), bank[t][:, 0:KC * P]).then_inc(xn2T_done, 1)
            act.wait_ge(shifted, 1)
            nc.scalar.activation(rp, rp, ACT.Exp).then_inc(routed, 1)

            def step(s):
                a = s
                if a.exists():
                    act.wait_ge(gu_mm, a.e + 1)
                    if a.from_(2):
                        act.wait_ge(hid_done, a.e - 1)
                    nc.scalar.activation(sil[a.slot % 2], bank[3 + a.slot % 2][:, 0:I], ACT.Silu).then_inc(silu_done, 1)
                a = s.plus(-2)
                if a.exists():
                    act.wait_ge(y_mm, a.e + 1)
                    if a.from_(Y_RING):
                        old = a.plus(-Y_RING)
                        act.wait_ge(y_out[old.slot], old.i * 16 + 16)
                    copy(y_sb[a.slot % Y_RING], bank[6 + a.slot % 2][:, 0:H]).then_inc(y_done, 1)
                a = s.plus(-1)
                if a.exists():
                    act.wait_ge(hid_turned, a.e + 1)
                    if a.from_(2):
                        act.wait_ge(y_mm, a.e - 1)
                    copy(hT[a.slot % 2], bank[5][0:I, 0:P]).then_inc(hT_done, 1)

            pipeline(act, step)

        @block.vector
        def _(dve):
            v = nc.vector
            steps = [0]

            def then(ins):
                steps[0] += 1
                ins.then_inc(dve_step, 1)
                dve.wait_ge(dve_step, steps[0])

            def norm_stats(tiles):
                for t in tiles:
                    last = v.bn_stats(stats[:, t, :], x_sb[:, t, :])
                then(last)
                for t in tiles:
                    last = v.bn_aggr(mv[:, t, :], stats[:, t, :])
                last.then_inc(var_done, 1)

            dve.wait_ge(consts, N_CONSTS)
            dve.wait_ge(x_in, 16)
            for t in range(TILES):
                then(v.bn_stats(stats[:, t, :], x_sb[:, t, :]))
            for t in range(TILES):
                last = v.bn_aggr(mv[:, t, :], stats[:, t, :])
            last.then_inc(var_done, 1)
            dve.wait_ge(turned, 1)
            v.tensor_copy(wkT[:, :, 0:HD], bank[1][0:L, 0:H].rearrange("p (h d) -> p h d", d=HD)).then_inc(wkvT_done, 1)
            v.tensor_copy(wvT, bank[1][0:L, H:2 * H]).then_inc(wkvT_done, 1)
            dve.wait_ge(std_done, 1)
            then(v.reciprocal(rstd[:], std[:]))
            for t in range(TILES):
                v.tensor_scalar(xn[:, t, :], x_sb[:, t, :], mv[:, t, 0:1], rstd[:, t:t + 1],
                                ALU.subtract, ALU.mult).then_inc(xn_done, 1)
            dve.wait_ge(turned, 3)
            for k in range(KC):
                last = v.tensor_scalar(wqT[:, k, :, 0:HD],
                                       bank[0][:, k * H:k * H + H].rearrange("p (h d) -> p h d", d=HD),
                                       -float(HD) ** -0.5, None, ALU.mult)
                if k == 0:
                    then(last)
            last.then_inc(wqT_done, 1)
            for g in range(4):
                if g % 2 == 0:
                    dve.wait_ge(k_mm, g + 1)
                    if g:
                        dve.wait_ge(k_done, g)
                    v.tensor_copy(kT[:, g, :], bank[4 + g][:]).then_inc(k_done, 1)
            dve.wait_ge(turned, 4)
            v.tensor_copy(xnT[:, 0, :], bank[2][:]).then_inc(xnT_done, 1)
            dve.wait_ge(v_mm, 1)
            for t in (0, 1):
                last = v.tensor_copy(v_sb[:, t, :, 0:HD], bank[0][:, (t % 2) * H:(t % 2) * H + H]
                                     .rearrange("p (h d) -> p h d", d=HD))
                if t == 0:
                    then(last)
            last.then_inc(v_done, 1)
            for g in (0, 2):
                dve.wait_ge(q_mm, g + 1)
                v.tensor_copy(qT[:, g, :], bank[4 + g][:]).then_inc(q_done, 1)

            def mask_scores(n):
                dve.wait_ge(scored, n + 1)
                if n >= 3:
                    dve.wait_ge(probs_turned, n - 2)
                for qt, cols in enumerate((slice(0, P), slice(P, 3 * P))):
                    v.tensor_tensor_reduce(score[n % 3][:, cols], bank[n % 4][:, cols], mask[:, cols], 1.0, BIG,
                                           ALU.add, ALU.min, rmin[:, n, qt:qt + 1]).then_inc(masked, 1)

            def normalise(b):
                dve.wait_ge(pv_done, NH * (b + 1))
                if b:
                    dve.wait_ge(dve_step, steps[0])
                for qt in range(QT):
                    o = bank[6 + qt][:, 0:NH * VW].rearrange("p (h w) -> p h w", w=VW)
                    last = v.reciprocal(o_rden[:, qt * NH:qt * NH + NH].unsqueeze(2), o[:, :, HD:VW])
                then(last)
                for qt in range(QT):
                    o = bank[6 + qt][:, 0:NH * VW].rearrange("p (h w) -> p h w", w=VW)
                    last = v.tensor_tensor(att[:, QT * b + qt, :].rearrange("p (h d) -> p h d", d=HD), o[:, :, 0:HD],
                                           o_rden[:, qt * NH:qt * NH + NH].unsqueeze(2).broadcast_to([P, NH, HD]),
                                           ALU.mult)
                last.then_inc(att_done, 1)

            for i in range(HEADS + 3):
                if i < HEADS:
                    mask_scores(i)
                n = i - 2
                if 0 <= n < HEADS and n % 2 == 1:
                    dve.wait_ge(probs_turned, n + 1)
                    if n >= 2:
                        dve.wait_ge(pv_done, n - 1)
                    v.tensor_copy(probT[1], bank[5][:, 0:3 * P]).then_inc(probT_dve, 1)
                if i == NH + 2:
                    normalise(0)
            normalise(1)

            dve.wait_ge(tanh_done, 1)
            for t in range(TILES):
                dve.wait_ge(projected, t + 1)
                v.scalar_tensor_tensor(out=x_sb[:, t, :], in0=bank[4 + t % 2][:, 0:H], scalar=tgates[:, 0:1],
                                       in1=x_sb[:, t, :], op0=ALU.mult, op1=ALU.add).then_inc(x1_done, 1)
                dve.wait_ge(x1_done, t + 1)
                then(v.bn_stats(stats[:, t, :], x_sb[:, t, :]))
                v.bn_aggr(mv[:, t, :], stats[:, t, :]).then_inc(var_done, 1)
            for t in range(TILES):
                dve.wait_ge(std_done, t + 2)
                then(v.reciprocal(rstd[:, t:t + 1], std[:, t:t + 1]))
                v.tensor_scalar(xn[:, t, :], x_sb[:, t, :], mv[:, t, 0:1], rstd[:, t:t + 1],
                                ALU.subtract, ALU.mult).then_inc(xn2_done, 1)

            dve.wait_ge(logits_done, TILES)
            logits = bank[6][:, 0:TILES * E].rearrange("p (t e) -> p t e", t=TILES)
            then(v.tensor_reduce(rstat[:, 0, :], logits, AX.X, ALU.max))
            v.tensor_tensor(rp, logits, rstat[:, 0, :].unsqueeze(2).broadcast_to([P, TILES, E]),
                            ALU.subtract).then_inc(shifted, 1)
            dve.wait_ge(routed, 1)
            then(v.tensor_reduce(rstat[:, 1, :], rp, AX.X, ALU.add))
            then(v.reciprocal(rstat[:, 1, :], rstat[:, 1, :]))
            then(v.tensor_tensor(rp, rp, rstat[:, 1, :].unsqueeze(2).broadcast_to([P, TILES, E]), ALU.mult))
            for t in range(TILES):
                last = v.max(top[:, t, :], rp[:, t, :])
            then(last)
            for t in range(TILES):
                last = v.match_replace(rp2[:, t, :], top[:, t, :], rp[:, t, :], -1.0)
            then(last)
            v.tensor_scalar(rselb, rp2, 0.0, None, ALU.is_lt).then_inc(selected, 1)
            v.tensor_scalar(rsel, rp2, 0.0, None, ALU.is_lt)
            then(v.tensor_reduce(rstat[:, 2, :], top, AX.X, ALU.add))
            then(v.reciprocal(rstat[:, 2, :], rstat[:, 2, :]))
            then(v.tensor_tensor(rp, rp, rstat[:, 2, :].unsqueeze(2).broadcast_to([P, TILES, E]), ALU.mult))
            dve.wait_ge(counted, 1)
            before = bank[7][:, 0:TILES * E].rearrange("p (t e) -> p t e", t=TILES)
            then(v.scalar_tensor_tensor(out=place1[:], in0=before, scalar=1.0, in1=rsel, op0=ALU.add, op1=ALU.mult))
            v.scalar_tensor_tensor(out=keep, in0=before, scalar=float(CAP), in1=rp, op0=ALU.is_lt, op1=ALU.mult)
            for t in range(TILES):
                last = v.scalar_tensor_tensor(out=row1[:, t, :], in0=before[:, t, :], scalar=float(CAP - 1),
                                              in1=expert_row1[:], op0=ALU.min, op1=ALU.add)
            then(last)
            then(v.tensor_tensor(row1, row1, rsel, ALU.mult))
            for t in range(TILES):
                last = v.max(row8f[:, t, :], row1[:, t, :])
            then(last)
            for t in range(TILES):
                then(v.tensor_tensor(match, row1[:, t, :].unsqueeze(1).broadcast_to([P, TOPK, E]),
                                     row8f[:, t, :].unsqueeze(2).broadcast_to([P, TOPK, E]), ALU.is_equal))
                then(v.tensor_tensor(match, match, keep[:, t, :].unsqueeze(1).broadcast_to([P, TOPK, E]), ALU.mult))
                then(v.tensor_reduce(w8[:, t, :], match, AX.X, ALU.add))
                v.tensor_scalar(row8[:, t, :], row8f[:, t, :], -1.0, None, ALU.add).then_inc(rows_ready, 1)

            def step(s):
                a = s.plus(LOOKAHEAD)
                if a.exists():
                    if a.from_(2):
                        dve.wait_ge(slots_mm, a.e - 1)
                    for t in range(TILES):
                        last = v.tensor_scalar(onehot[a.slot % 2][:, t, :], slot1[:],
                                               place1[:].rearrange("p t e -> p (t e)")[:, bass.ds(a.e + t * E, 1)],
                                               None, ALU.is_equal)
                    last.then_inc(onehot_done, 1)
                a = s.plus(LOOKAHEAD - 1)
                if a.exists():
                    dve.wait_ge(slots_mm, a.e + 1)
                    if a.from_(UNROLL):
                        dve.wait_ge(xe_in[a.slot], a.i * 16)
                    v.tensor_scalar(slot_token[:, a.slot:a.slot + 1], bank[0][:, 0:1], float(NO_TOKEN),
                                    bank[0][:, 1:2], ALU.add, ALU.add).then_inc(slots_done, 1)
                a = s.plus(1)
                if a.exists():
                    dve.wait_ge(xe_turned, a.e + 1)
                    if a.from_(2):
                        dve.wait_ge(gu_mm, a.e - 1)
                    v.tensor_copy(xeT[a.slot % 2].rearrange("p k t -> p (k t)"),
                                  bank[1 + a.slot % 2][:, 0:KC * P]).then_inc(xeT_done, 1)
                a = s
                if a.exists():
                    dve.wait_ge(silu_done, a.e + 1)
                    if a.from_(2):
                        dve.wait_ge(hid_turned, a.e - 1)
                    v.tensor_tensor(hid[a.slot % 2], sil[a.slot % 2], bank[3 + a.slot % 2][:, I:2 * I],
                                    ALU.mult).then_inc(hid_done, 1)

            pipeline(dve, step)

            def sum_rows(t, first):
                for k in range(TOPK):
                    dve.wait_ge(c_in[k], t * 16 + 16)
                    w = w8[:].rearrange("p t k -> p (t k)")[:, bass.ds(t * TOPK + k, 1)]
                    a = acc[:, bass.ds(t, 1), :].rearrange("p a n -> p (a n)")
                    if k == 0:
                        v.tensor_scalar(a, c_sb[:, k, :], w, None, ALU.mult).then_inc(combined, 1)
                    else:
                        dve.wait_ge(combined, t * TOPK + k)
                        v.scalar_tensor_tensor(out=a, in0=c_sb[:, k, :], scalar=w, in1=a,
                                               op0=ALU.mult, op1=ALU.add).then_inc(combined, 1)
                dve.wait_ge(combined, t * TOPK + TOPK)
                v.scalar_tensor_tensor(out=xn[:, bass.ds(t, 1), :].rearrange("p a n -> p (a n)"),
                                       in0=acc[:, bass.ds(t, 1), :].rearrange("p a n -> p (a n)"),
                                       scalar=tgates[:, 1:2],
                                       in1=x_sb[:, bass.ds(t, 1), :].rearrange("p a n -> p (a n)"),
                                       op0=ALU.mult, op1=ALU.add).then_inc(out_done, 1)

            with dve.Fori(0, TILES) as t:
                sum_rows(t, False)


_INS = ['x', 'ctx_512', 'g_xattn', 'g_ffn', 'L0_xattn_Wq', 'L0_xattn_Wkv_expand', 'L0_xattn_Wout',
        'L0_ffn_router_weight', 'L0_ffn_gate_up_proj', 'L0_ffn_down_proj']
_OUTS = [((B, S, H), 'float32')]


def kernel(**inputs):
    import numpy as _np
    import concourse.bacc as _bacc
    from concourse import mybir as _mybir
    from concourse.bass_utils import run_bass_kernel_spmd as _run

    nc = _bacc.Bacc("TRN2", target_bir_lowering=False, num_devices=1)
    arrays, args = {}, []
    for name in _INS:
        a = _np.ascontiguousarray(inputs[name])
        arrays[f"in_{name}_dram"] = a
        args.append(nc.dram_tensor(f"in_{name}_dram", a.shape, _mybir.dt.from_np(a.dtype), kind="ExternalInput").ap())
    for i, (shape, dtype) in enumerate(_OUTS):
        dt = _mybir.dt.from_np(_np.dtype(dtype))
        args.append(nc.dram_tensor(f"out_{i}_dram", shape, dt, kind="ExternalOutput").ap())
    flamingo_moe(nc, *args)
    r = _run(nc, [arrays], core_ids=[0])
    got = tuple(r.results[0][f"out_{i}_dram"] for i in range(len(_OUTS)))
    return got[0]
```

```python
from contextlib import ExitStack

import concourse.bass as bass
from concourse import mybir

ALU = mybir.AluOpType
ACT = mybir.ActivationFunctionType
AX = mybir.AxisListType
F32 = mybir.dt.float32
BF16 = mybir.dt.bfloat16
F32R = mybir.dt.float32r
U32 = mybir.dt.uint32

P = 128
B, S, H = 2, 256, 256
NH, HD, L = 16, 16, 64
E, I, TOPK, CAP = 64, 96, 8, 128
TILES = B * S // P
QT = S // P
KC = H // P
HP = 32
GROUPS = NH * HD // P
RESERVED = 32
HEADS = B * NH
EPS = 1e-5
BIG = 1e30
WORK = 4352
FAR = 16384
NO_TOKEN = 1024
IDS = 5
XE_RING = Y_RING = 4
UNROLL = 4
LOOKAHEAD = 8
EARLY = 40
CHUNK = 4
SCORES = 4
ROWS = TILES * TOPK
ADDS_FROM = EARLY + 4
TWO_ADDS_FROM = 56


class Expert:

    def __init__(self, i, u):
        self.i, self.slot = i + u // UNROLL, u % UNROLL
        self.e = self.i * UNROLL + self.slot
        self.static = isinstance(self.i, int)

    def plus(self, d):
        return Expert(self.i, self.slot + d)

    def from_(self, first):
        return not self.static or self.e >= first

    def exists(self):
        return not self.static or 0 <= self.e < E


def pipeline(eng, step, before_reserved=lambda: None):
    for s in range(-LOOKAHEAD, UNROLL):
        step(Expert(0, s), False)
    with eng.Fori(1, RESERVED // UNROLL) as i:
        for u in range(UNROLL):
            step(Expert(i, u), False)
    before_reserved()
    with eng.Fori(RESERVED // UNROLL, EARLY // UNROLL) as i:
        for u in range(UNROLL):
            step(Expert(i, u), False)
    for s in range(EARLY, EARLY + 2 * UNROLL):
        step(Expert(0, s), True)
    with eng.Fori(EARLY // UNROLL + 2, (E - LOOKAHEAD) // UNROLL) as i:
        for u in range(UNROLL):
            step(Expert(i, u), True)
    for s in range(E - LOOKAHEAD, E + 3):
        step(Expert(0, s), True)


def flamingo_moe(nc, x, ctx_kv, g_xattn, g_ffn, wq, wkv, wout, router, gate_up, down, out):
    with ExitStack() as stack:
        def sb(name, shape, dt=F32):
            return stack.enter_context(nc.sbuf_tensor(name, shape, dt))

        def sem(name):
            return stack.enter_context(nc.semaphore(name))

        bank = [stack.enter_context(nc.psum_tensor(f"bank{i}", [P, 512], F32)) for i in range(8)]
        xn2_dram = nc.dram_tensor("xn2_dram", (TILES * P, H), F32, kind="Internal").ap()
        ye_dram = nc.dram_tensor("ye_dram", (EARLY * CAP, H), F32, kind="Internal").ap()

        gate_w = sb("gate_w", [P, E, KC * 2 * I])
        down_w = sb("down_w", [I, E, H])
        x_sb = sb("x_sb", [P, TILES, H])
        xn = sb("xn", [P, TILES, H])
        ident = sb("ident", [P, P])
        mask = sb("mask", [P, 3 * P])
        slot1 = sb("slot1", [P, P], BF16)
        earlier = sb("earlier", [P, P], BF16)
        ones = sb("ones", [P, P], BF16)
        tokens = sb("tokens", [P, TILES * P])
        ids = sb("ids", [P, TILES, E, IDS], BF16)
        gates = sb("gates", [P, 2])
        head_rows = sb("head_rows", [P, P // HD])
        tgates = sb("tgates", [P, 2])
        eps = sb("eps", [P, 1])
        stats = sb("stats", [P, TILES, 6])
        mv = sb("mv", [P, TILES, 2])
        std = sb("std", [P, TILES])
        rstd = sb("rstd", [P, TILES])
        rmin = sb("rmin", [P, HEADS, QT])
        rsum = sb("rsum", [P, HEADS, QT])
        rrec = sb("rrec", [P, HEADS, QT])
        place1 = sb("place1", [P, TILES, E])
        slot_token = sb("slot_token", [P, E], U32)
        slot_weight = sb("slot_weight", [P, E])
        row8 = sb("row8", [P, ROWS], U32)
        router_sb = sb("router_sb", [E, H])
        rT = sb("rT", [P, KC, E])
        expert_far = sb("expert_far", [P, EARLY])
        xe = sb("xe", [P, XE_RING, H])
        scatter = sb("scatter", [P, TILES * P], F32R)
        y_high = sb("y_high", [P, H], F32R)
        y_low = sb("y_low", [P, H], F32R)
        work = sb("work", [P, WORK])

        def carver(tensor, words):
            used = [0]

            def take(n, dt=F32, parts=P):
                a = tensor[0:parts, used[0]:used[0] + n]
                used[0] += n
                assert used[0] <= words
                return a if dt == F32 else a.bitcast(dt)
            return take

        def carver(tensor, words):
            used = [0]

            def take(n, dt=F32, parts=P):
                a = tensor[0:parts, used[0]:used[0] + n]
                used[0] += n
                assert used[0] <= words
                return a if dt == F32 else a.bitcast(dt)
            return take

        take = carver(gate_w[:, RESERVED:E, :].rearrange("p e n -> p (e n)"), (E - RESERVED) * KC * 2 * I)
        qT = take(GROUPS * B * S).rearrange("p (g t) -> p g t", g=GROUPS)
        kT = take(NH * B * S).rearrange("p (h t) -> p h t", h=NH)
        v_sb = take(TILES * NH * HP).rearrange("p (t h w) -> p t h w", t=TILES, w=HP)
        xnT = take(KC * B * S).rearrange("p (k t) -> p k t", k=KC)
        take = carver(xe[:].rearrange("p r n -> p (r n)"), XE_RING * H)
        wqT = take(KC * H).rearrange("p (k n) -> p k n", k=KC)
        ctxT = take(B * S, parts=L)
        take = carver(work, WORK)
        wq_sb = take(KC * H).rearrange("p (o i) -> p o i", o=KC)
        wkv_sb = take(4 * L).rearrange("p (r l) -> p r l", r=4)
        ctx_sb = take(TILES * L).rearrange("p (t l) -> p t l", t=TILES)
        wout_sb = take(KC * H).rearrange("p (o i) -> p o i", o=KC)
        wout_pad = take(KC * NH * HP).rearrange("p (o h d) -> p o h d", o=KC, d=HP)
        wkT = take(H, parts=L)
        wvT = take(H, parts=L)
        take(H)
        woT = take(4 * H).rearrange("p (g n) -> p g n", g=4)
        take = carver(work, WORK)
        take(4 * S)
        score = [take(3 * P) for _ in range(SCORES)]
        probT = [take(3 * P) for _ in range(2)]
        take = carver(work, WORK)
        attT = take(4 * S).rearrange("p (g t) -> p g t", g=4)
        xn2T = [take(KC * P).rearrange("p (k t) -> p k t", k=KC) for _ in range(2)]
        take = carver(work, WORK)
        onehot = [take(TILES * P // 2, BF16).rearrange("p (t s) -> p t s", t=TILES) for _ in range(2)]
        y_sb = [take(H) for _ in range(Y_RING)]
        xeT = [take(KC * P).rearrange("p (k t) -> p k t", k=KC) for _ in range(2)]
        sil = [take(I) for _ in range(2)]
        hid = [take(I) for _ in range(2)]
        hT = [take(P, parts=I) for _ in range(2)]
        take(2816 - 2688)
        rp = take(TILES * E).rearrange("p (t e) -> p t e", t=TILES)
        rp2 = take(TILES * E).rearrange("p (t e) -> p t e", t=TILES)
        rrest = take(TILES * E).rearrange("p (t e) -> p t e", t=TILES)
        rselb = take(TILES * E // 2, BF16).rearrange("p (t e) -> p t e", t=TILES)
        top = take(TILES * TOPK).rearrange("p (t k) -> p t k", t=TILES)
        rstat = take(4 * TILES).rearrange("p (n t) -> p n t", n=4)
        valid = take(TILES * EARLY).rearrange("p (t e) -> p t e", t=TILES)
        far = take(TILES * EARLY).rearrange("p (t e) -> p t e", t=TILES)
        far8 = take(ROWS).rearrange("p (t k) -> p t k", t=TILES)
        C_EXPERTS = -(-ROWS * H // (KC * 2 * I))
        c_sb = gate_w[:, 0:C_EXPERTS, :].rearrange("p e n -> p (e n)")[:, 0:ROWS * H].rearrange(
            "p (r n) -> p r n", r=ROWS)

        x_in, wq_in, ctx_in, wkv_in, wout_in, router_in, gates_in = (
            sem(n) for n in ("x_in", "wq_in", "ctx_in", "wkv_in", "wout_in", "router_in", "gates_in"))
        gate_w_in, gate_w_late_in, down_w_in = sem("gate_w_in"), sem("gate_w_late_in"), sem("down_w_in")
        ident_built, eps_built, v_padded, consts = sem("ident_built"), sem("eps_built"), sem("v_padded"), sem("consts")
        heads_built, k_act, k_dve, xe_cleared = sem("heads_built"), sem("k_act"), sem("k_dve"), sem("xe_cleared")
        turned = sem("turned")
        wqT_done, wkvT_done, ctxT_done, woT_done, rT_done = (
            sem(n) for n in ("wqT_done", "wkvT_done", "ctxT_done", "woT_done", "rT_done"))
        wout_padded = sem("wout_padded")
        xn_done, xnT_done = sem("xn_done"), sem("xnT_done")
        std_done, var_done = sem("std_done"), sem("var_done")
        k_mm, v_mm, v_done, q_mm, q_done = sem("k_mm"), sem("v_mm"), sem("v_done"), sem("q_mm"), sem("q_done")
        scored, masked, exped, probs_turned = (sem(n) for n in ("scored", "masked", "exped", "probs_turned"))
        inverted, scaled = sem("inverted"), sem("scaled")
        probT_act, probT_dve, pv_done = (sem(n) for n in ("probT_act", "probT_dve", "pv_done"))
        attT_done, projected, x1_done = (sem(n) for n in ("attT_done", "projected", "x1_done"))
        tanh_done, xn2_done, xn2_stored = sem("tanh_done"), sem("xn2_done"), sem("xn2_stored")
        xn2_turned, xn2T_done, logits_done = sem("xn2_turned"), sem("xn2T_done"), sem("logits_done")
        shifted, routed, selected, counted, placed = (
            sem(n) for n in ("shifted", "routed", "selected", "counted", "placed"))
        onehot_done, slots_mm, slots_done, rows_ready = (
            sem(n) for n in ("onehot_done", "slots_mm", "slots_done", "rows_ready"))
        xe_in = [sem(f"xe_in{i}") for i in range(XE_RING)]
        xe_turned, xeT_done, gu_mm, silu_done, hid_done, hid_turned, hT_done, y_mm, y_done = (
            sem(n) for n in ("xe_turned", "xeT_done", "gu_mm", "silu_done", "hid_done", "hid_turned",
                             "hT_done", "y_mm", "y_done"))
        y_out = [sem(f"y_out{i}") for i in range(Y_RING)]
        y_high_done, y_low_done, scatter_done, scattered = (
            sem(n) for n in ("y_high_done", "y_low_done", "scatter_done", "scattered"))
        c_cleared = sem("c_cleared")
        c_in = [sem(f"c_in{i}") for i in range(TILES)]
        added, out_done, stored = sem("added"), sem("out_done"), sem("stored")
        dve_step = sem("dve_step")
        n_consts = [0]

        x_tiles = x.rearrange("b (t p) h -> p (b t) h", p=P)
        out_tiles = out.rearrange("b (t p) h -> p (b t) h", p=P)
        block = stack.enter_context(nc.Block())

        @block.sync
        def _(sp):
            sp.dma_start(x_sb[:], x_tiles).then_inc(x_in, 16)
            sp.dma_start(wkv_sb, wkv.rearrange("(r p) l -> p r l", p=P)).then_inc(wkv_in, 16)
            for b in range(B):
                sp.dma_start(ctx_sb[:, QT * b:QT * b + QT, :],
                             ctx_kv[b, 0:S, :].rearrange("(t p) l -> p t l", p=P)).then_inc(ctx_in, 16)
            sp.dma_start(wq_sb, wq.rearrange("(o p) i -> p o i", p=P)).then_inc(wq_in, 16)
            sp.dma_start(gates[:, 0:1], g_xattn.partition_broadcast(P)).then_inc(gates_in, 16)
            sp.dma_start(gates[:, 1:2], g_ffn.partition_broadcast(P)).then_inc(gates_in, 16)
            sp.dma_start(wout_sb[:], wout.rearrange("(o p) i -> p o i", p=P)).then_inc(wout_in, 16)
            sp.dma_start(router_sb[:], router).then_inc(router_in, 16)

            def load_gate(e, signal):
                sp.dma_start(gate_w[:, e:e + CHUNK, :],
                             gate_up[e:e + CHUNK].rearrange("e (p c) f -> p e (c f)", c=KC)).then_inc(signal, 16)

            for e in range(0, E, CHUNK):
                if e < RESERVED:
                    load_gate(e, gate_w_in)
                sp.dma_start(down_w[:, e:e + CHUNK, :],
                             down[e:e + CHUNK].rearrange("e i h -> i e h")).then_inc(down_w_in, 16)
            sp.wait_ge(pv_done, HEADS)
            for t in range(TILES):
                sp.wait_ge(xn2_done, t + 1)
                sp.dma_start(xn2_dram[t * P:t * P + P, :], xn[:, t, :]).then_inc(xn2_stored, 16)
            for e in range(RESERVED, E, CHUNK):
                load_gate(e, gate_w_late_in)

            with sp.Fori(0, EARLY // UNROLL) as i:
                for u in range(UNROLL):
                    e = Expert(i, u)
                    sp.wait_ge(y_done, e.e + 1)
                    sp.dma_start(ye_dram.rearrange("(e s) h -> s e h", s=CAP)[:, bass.ds(e.e, 1), :]
                                 .rearrange("s a h -> s (a h)"), y_sb[u]).then_inc(y_out[u], 16)
            for t in range(TILES):
                sp.wait_ge(out_done, t + 1)
                sp.dma_start(out_tiles[:, t, :], xn[:, t, :]).then_inc(stored, 16)
            sp.wait_ge(stored, 16 * TILES)

        @block.gpsimd
        def _(pool):
            def const(ins):
                n_consts[0] += 1
                ins.then_inc(consts, 1)

            pool.memset(ident[:], 0.0).then_inc(ident_built, 1)
            pool.wait_ge(ident_built, 1)
            pool.affine_select(out=ident[:], in_=ident[:], compare_op=ALU.not_equal, fill=1.0, base=0,
                               pattern=[[-1, P]], channel_multiplier=1).then_inc(ident_built, 1)
            pool.memset(head_rows[:], 1.0).then_inc(heads_built, 1)
            pool.wait_ge(heads_built, 1)
            pool.affine_select(out=head_rows[:], in_=head_rows[:], compare_op=ALU.is_ge, fill=0.0, base=0,
                               pattern=[[-HD, P // HD]], channel_multiplier=1).then_inc(heads_built, 1)
            pool.wait_ge(heads_built, 2)
            pool.affine_select(out=head_rows[:], in_=head_rows[:], compare_op=ALU.is_ge, fill=0.0, base=HD - 1,
                               pattern=[[HD, P // HD]], channel_multiplier=-1).then_inc(heads_built, 1)
            pool.memset(eps[:], EPS).then_inc(eps_built, 1)
            pool.memset(v_sb[:, :, :, HD:HP], 0.0).then_inc(v_padded, 1)
            const(pool.memset(wout_pad[:, :, :, HD:HP], 0.0))
            pool.wait_ge(wout_in, 16)
            for o in range(KC):
                pool.tensor_copy(wout_pad[:, o, :, 0:HD],
                                 wout_sb[:, o, :].rearrange("p (h d) -> p h d", d=HD)).then_inc(wout_padded, 1)
            const(pool.memset(mask[:], 0.0))
            const(pool.memset(ones[:], 1.0))
            pool.wait_ge(consts, n_consts[0])
            for c in (0, 2):
                const(pool.affine_select(out=mask[:, c * P:c * P + P], in_=mask[:, c * P:c * P + P],
                                         compare_op=ALU.is_ge, fill=BIG, base=0, pattern=[[-1, P]],
                                         channel_multiplier=1))
            const(pool.affine_select(out=earlier[:], in_=ones[:], compare_op=ALU.is_gt, fill=0.0, base=0,
                                     pattern=[[1, P]], channel_multiplier=-1))

            def count_up(out, pattern, base, per_partition):
                const(pool.iota(out, pattern=pattern, base=base, channel_multiplier=per_partition,
                                allow_small_or_imprecise_dtypes=True))

            count_up(slot1[:], [[1, P]], 1, 0)
            count_up(ids[:, :, :, 0], [[0, TILES], [0, E]], 0, 1)
            count_up(ids[:, :, :, 1], [[P, TILES], [0, E]], -NO_TOKEN, 0)
            count_up(tokens[:], [[1, TILES * P]], 0, 0)
            count_up(expert_far[:], [[-CAP, EARLY]], FAR, 0)

            for n in range(HEADS):
                pool.wait_ge(inverted, n + 1)
                for qt, cols in enumerate((slice(0, P), slice(P, 3 * P))):
                    part = score[n % SCORES][:, cols]
                    pool.tensor_scalar(part, part, rrec[:, n, qt:qt + 1], 1.0, ALU.mult, ALU.mult).then_inc(scaled, 1)

            pool.wait_ge(pv_done, HEADS)
            pool.memset(xe[:], 0.0).then_inc(xe_cleared, 1)
            pool.wait_ge(xe_cleared, 1)
            pool.wait_ge(xn2_stored, 16 * TILES)
            last_token, last_row = pool.to_reg(TILES * P - 1), pool.to_reg(EARLY * CAP - 1)

            def gather_tokens(e):
                pool.wait_ge(slots_done, e + 1)
                if e >= XE_RING:
                    pool.wait_ge(xe_turned, e - XE_RING + 1)
                pool.indirect_dma_start(
                    out=xe[:, e % XE_RING, :], out_offset=None, in_=xn2_dram,
                    in_offset=bass.IndirectOffsetOnAxis(ap=slot_token[:, e:e + 1], axis=0),
                    bounds_check=last_token, oob_is_err=False).then_inc(xe_in[e % XE_RING], 16)

            def gather_rows(c):
                if c == 0:
                    for r in range(Y_RING):
                        pool.wait_ge(y_out[r], 16 * (EARLY // Y_RING))
                    pool.wait_ge(rows_ready, 1)
                    pool.wait_ge(c_cleared, ROWS)
                t, k = c % TILES, c // TILES
                if k:
                    pool.wait_ge(c_in[t], 16 * k)
                pool.indirect_dma_start(
                    out=c_sb[:, c, :], out_offset=None, in_=ye_dram,
                    in_offset=bass.IndirectOffsetOnAxis(ap=row8[:, t * TOPK + k:t * TOPK + k + 1], axis=0),
                    bounds_check=last_row, oob_is_err=False).then_inc(c_in[t], 16)

            clear_from = EARLY - ROWS // 2 + 2
            c = 0
            for e in range(E):
                gather_tokens(e)
                if 0 <= e - clear_from < ROWS // 2:
                    pool.wait_ge(gu_mm, C_EXPERTS)
                    for n in (2 * (e - clear_from), 2 * (e - clear_from) + 1):
                        pool.memset(c_sb[:, n, :], 0.0).then_inc(c_cleared, 1)
                if e >= EARLY + 5:
                    for _ in range(1 + (e % 3 == 0)):
                        gather_rows(c)
                        c += 1
            while c < ROWS:
                gather_rows(c)
                c += 1

        @block.tensor
        def _(pe):
            def turn_blocks(pairs, signal):
                for src, d in pairs:
                    k, m = src.shape
                    last = nc.tensor.transpose(d, src, ident[0:k, 0:k])
                last.then_inc(signal, 1)

            pe.wait_ge(ident_built, 2)
            pe.wait_ge(wkv_in, 16)
            turn_blocks([(wkv_sb[:, r, :], bank[1][0:L, r * P:r * P + P]) for r in range(4)], turned)
            pe.wait_ge(ctx_in, 32)
            turn_blocks([(ctx_sb[:, t, :], bank[2][0:L, t * P:t * P + P]) for t in range(TILES)], turned)
            pe.wait_ge(wq_in, 16)
            turn_blocks([(wq_sb[:, o, k * P:k * P + P], bank[0][:, (k * KC + o) * P:(k * KC + o + 1) * P])
                         for k in range(KC) for o in range(KC)], turned)
            pe.wait_ge(wkvT_done, 2)
            pe.wait_ge(ctxT_done, 1)
            for g in range(GROUPS):
                nc.tensor.matmul(bank[4 + g][:], wkT[:, g * P:g * P + P], ctxT, start=True, stop=True).then_inc(k_mm, 1)
            pe.wait_ge(router_in, 16)
            turn_blocks([(router_sb[:, k * P:k * P + P], bank[3][:, k * E:k * E + E]) for k in range(KC)], turned)
            pe.wait_ge(wqT_done, 1)
            for t in range(TILES):
                last = nc.tensor.matmul(bank[t // 2][:, (t % 2) * H:(t % 2) * H + H], ctxT[:, t * P:t * P + P], wvT,
                                        start=True, stop=True)
                if t % 2:
                    last.then_inc(v_mm, 1)
            pe.wait_ge(xn_done, TILES)
            pe.wait_ge(rT_done, 1)
            for k in range(KC):
                turn_blocks([(xn[:, t, k * P:k * P + P], bank[2 + k][:, t * P:t * P + P])
                             for t in range(TILES)], turned)
            pe.wait_ge(wout_padded, KC)
            pe.wait_ge(v_done, 2)
            for o in range(KC):
                turn_blocks([(wout_pad[:, o, 4 * g:4 * g + 4, :].rearrange("p h d -> p (h d)"),
                              bank[o][:, g * P:g * P + P]) for g in range(4)], turned)
            pe.wait_ge(xnT_done, KC)
            for g in range(GROUPS):
                for k in range(KC):
                    last = nc.tensor.matmul(bank[6 + g][:], wqT[:, k, g * P:g * P + P], xnT[:, k, :],
                                            start=(k == 0), stop=(k == KC - 1))
                last.then_inc(q_mm, 1)
            pe.wait_ge(woT_done, KC)
            pe.wait_ge(k_act, NH // 2)
            pe.wait_ge(k_dve, NH // 2)
            pe.wait_ge(q_done, GROUPS)
            pe.wait_ge(v_padded, 1)

            def scores(n):
                b, h = n // NH, n % NH
                g, j = h // (NH // GROUPS), n % 4
                if n >= 4:
                    pe.wait_ge(masked, 2 * (n - 3))
                nc.tensor.matmul(bank[j][:, 0:P], qT[:, g, b * S:b * S + P], kT[:, h, b * S:b * S + P],
                                 start=True, stop=True)
                nc.tensor.matmul(bank[j][:, P:3 * P], qT[:, g, b * S + P:b * S + S], kT[:, h, b * S:b * S + S],
                                 start=True, stop=True).then_inc(scored, 1)

            def turn_probs(n):
                pe.wait_ge(scaled, 2 * n + 2)
                if n >= 2:
                    pe.wait_ge(probT_act if n % 2 == 0 else probT_dve, (n - 2) // 2 + 1)
                for c in range(3):
                    last = nc.tensor.transpose(bank[4 + n % 2][:, c * P:c * P + P],
                                               score[n % SCORES][:, c * P:c * P + P], ident[:])
                last.then_inc(probs_turned, 1)

            def turn_of(group):
                return group + (group > QT * 2)

            def values(n):
                b, h = n // NH, n % NH
                group, j = n // 4, n % 4
                pe.wait_ge(probT_act if n % 2 == 0 else probT_dve, n // 2 + 1)
                if j == 0:
                    turn = turn_of(group)
                    if turn == 7:
                        pe.wait_ge(x1_done, QT)
                    elif turn >= 2:
                        pe.wait_ge(attT_done, group - 1 if turn < 6 else group)
                o = bank[6 + turn_of(group) % 2]
                rows = slice(HP * j, HP * j + HP)
                pt = probT[n % 2]
                nc.tensor.matmul(o[rows, 0:S], v_sb[:, QT * b, h, :], pt[:, 0:2 * P], start=True, stop=False,
                                 skip_group_check=True)
                nc.tensor.matmul(o[rows, P:S], v_sb[:, QT * b + 1, h, :], pt[:, 2 * P:3 * P], start=False,
                                 stop=True, skip_group_check=True).then_inc(pv_done, 1)

            def project(b):
                pe.wait_ge(attT_done, 4 * (b + 1))
                for qt in range(QT):
                    for g in range(4):
                        last = nc.tensor.matmul(bank[7][:, qt * H:qt * H + H], attT[:, g, qt * P:qt * P + P],
                                                woT[:, g, :], start=(g == 0), stop=(g == 3))
                last.then_inc(projected, 1)

            for i in range(HEADS + 4):
                if i < HEADS:
                    scores(i)
                if 0 <= i - 3 < HEADS:
                    turn_probs(i - 3)
                if i >= 4:
                    values(i - 4)
                if i - 4 == NH + 1:
                    project(0)
            project(1)

            pe.wait_ge(consts, n_consts[0])
            pe.wait_ge(masked, 2 * HEADS)
            for t in range(TILES):
                pe.wait_ge(xn2_done, t + 1)
                turn_blocks([(xn[:, t, k * P:k * P + P], bank[t][:, k * P:k * P + P]) for k in range(KC)],
                            xn2_turned)
            for t in range(TILES):
                pe.wait_ge(xn2T_done, t + 1)
                for k in range(KC):
                    last = nc.tensor.matmul(bank[6][:, t * E:t * E + E], xn2T[t % 2][:, k, :], rT[:, k, :],
                                            start=(k == 0), stop=(k == KC - 1))
                last.then_inc(logits_done, 1)
            pe.wait_ge(selected, 1)
            for t in range(TILES):
                for q in range(t + 1):
                    last = nc.tensor.matmul(bank[7][:, t * E:t * E + E], earlier[:] if q == t else ones[:],
                                            rselb[:, q, :], start=(q == 0), stop=(q == t))
            last.then_inc(counted, 1)

            pe.wait_ge(gate_w_in, 16 * (RESERVED // CHUNK))
            pe.wait_ge(down_w_in, 16 * (E // CHUNK))

            def step(s, late_part):
                a = s.plus(LOOKAHEAD - 1)
                if a.exists():
                    pe.wait_ge(onehot_done, a.e + 1)
                    if a.from_(1):
                        pe.wait_ge(slots_done, a.e)
                    for t in range(TILES):
                        last = nc.tensor.matmul(bank[0][:, 0:IDS], onehot[a.slot % 2][:, t, :],
                                                ids[:, t, bass.ds(a.e, 1), :].rearrange("p a n -> p (a n)"),
                                                start=(t == 0), stop=(t == TILES - 1))
                    last.then_inc(slots_mm, 1)
                a = s.plus(1)
                if a.exists():
                    pe.wait_ge(xe_in[a.slot], a.i * 16 + 16)
                    if a.from_(1):
                        pe.wait_ge(xeT_done, a.e)
                    rows = xe[:, a.slot, :].rearrange("s (p c) -> s c p", c=KC)
                    for c in range(KC):
                        last = nc.tensor.transpose(bank[1][:, c * P:c * P + P], rows[:, c, :], ident[:])
                    last.then_inc(xe_turned, 1)
                a = s
                if a.exists():
                    pe.wait_ge(xeT_done, a.e + 1)
                    if a.from_(2):
                        pe.wait_ge(hid_done, a.e - 1)
                    w = gate_w[:, bass.ds(a.e, 1), :].rearrange("p a n -> p (a n)")
                    for c in range(KC):
                        last = nc.tensor.matmul(bank[3 + a.slot % 2][:, 0:2 * I], xeT[a.slot % 2][:, c, :],
                                                w[:, c * 2 * I:(c + 1) * 2 * I], start=(c == 0), stop=(c == KC - 1))
                    last.then_inc(gu_mm, 1)
                a = s.plus(-3)
                if late_part and a.exists() and a.from_(EARLY):
                    pe.wait_ge(scatter_done, a.e - (EARLY - 1))
                    pe.wait_ge(y_low_done, a.e - (EARLY - 1))
                    first, final = a.static and a.e == EARLY, a.static and a.e == E - 1
                    if first:
                        pe.wait_ge(rows_ready, 1)
                    for t in range(TILES):
                        for part in (y_high, y_low):
                            last = nc.tensor.matmul(bank[6 + t // 2][:, (t % 2) * H:(t % 2) * H + H],
                                                    scatter[:, t * P:t * P + P], part[:],
                                                    start=first and t % 2 == 0 and part is y_high,
                                                    stop=final and part is y_low, skip_group_check=True)
                    last.then_inc(scattered, 1)
                a = s.plus(-2)
                if a.exists():
                    pe.wait_ge(hT_done, a.e + 1)
                    if late_part and a.from_(EARLY + 1):
                        pe.wait_ge(y_low_done, a.e - EARLY)
                    elif a.from_(1):
                        pe.wait_ge(y_done, a.e)
                    w = down_w[:, bass.ds(a.e, 1), :].rearrange("p a n -> p (a n)")
                    nc.tensor.matmul(bank[2][:, 0:H], hT[a.slot % 2], w, start=True, stop=True).then_inc(y_mm, 1)
                a = s.plus(-1)
                if a.exists():
                    pe.wait_ge(hid_done, a.e + 1)
                    if a.from_(1):
                        pe.wait_ge(hT_done, a.e)
                    nc.tensor.transpose(bank[5][0:I, 0:P], hid[a.slot % 2], ident[:]).then_inc(hid_turned, 1)

            pipeline(pe, step, lambda: pe.wait_ge(gate_w_late_in, 16 * ((E - RESERVED) // CHUNK)))

        @block.scalar
        def _(act):
            copy = nc.scalar.copy
            act.wait_ge(turned, 2)
            copy(ctxT, bank[2][0:L, :]).then_inc(ctxT_done, 1)
            act.wait_ge(eps_built, 1)
            act.wait_ge(var_done, 1)
            nc.scalar.activation(std[:], mv[:, :, 1], ACT.Sqrt, bias=eps[:]).then_inc(std_done, 1)

            act.wait_ge(heads_built, 3)
            act.wait_ge(k_mm, 2)
            for h in range(NH // 2, NH):
                nc.scalar.activation(kT[:, h, :], bank[5][:], ACT.Copy,
                                     scale=head_rows[:, h % (P // HD):h % (P // HD) + 1]).then_inc(k_act, 1)
            act.wait_ge(turned, 4)
            copy(rT[:].rearrange("p k n -> p (k n)"), bank[3][:, 0:KC * E]).then_inc(rT_done, 1)
            act.wait_ge(v_mm, 2)
            copy(v_sb[:, QT:2 * QT, :, 0:HD],
                 bank[1][:].rearrange("p (t h d) -> p t h d", t=QT, d=HD)).then_inc(v_done, 1)
            act.wait_ge(turned, 6)
            copy(xnT[:, 1, :], bank[3][:]).then_inc(xnT_done, 1)
            for o in range(KC):
                act.wait_ge(turned, 7 + o)
                copy(woT[:, :, o * P:o * P + P], bank[o][:].rearrange("p (g n) -> p g n", g=4)).then_inc(woT_done, 1)
            act.wait_ge(q_mm, 2)
            copy(qT[:, 1, :], bank[7][:]).then_inc(q_done, 1)
            act.wait_ge(gates_in, 32)
            nc.scalar.activation(tgates[:], gates[:], ACT.Tanh).then_inc(tanh_done, 1)

            for i in range(HEADS + 5):
                if i < HEADS:
                    for qt in range(QT):
                        act.wait_ge(masked, 2 * i + qt + 1)
                        part = score[i % SCORES][:, 0:P] if qt == 0 else score[i % SCORES][:, P:3 * P]
                        nc.scalar.activation(part, part, ACT.Exp, bias=rmin[:, i, qt:qt + 1], scale=-1.0,
                                             accum_out=rsum[:, i, qt:qt + 1]).then_inc(exped, 1)
                n = i - 3
                if 0 <= n < HEADS and n % 2 == 0:
                    act.wait_ge(probs_turned, n + 1)
                    if n >= 2:
                        act.wait_ge(pv_done, n - 1)
                    copy(probT[0], bank[4][:, 0:3 * P]).then_inc(probT_act, 1)
                if i >= 8 and i % 4 == 0:
                    group = i // 4 - 2
                    act.wait_ge(pv_done, 4 * group + 4)
                    if group >= 4:
                        act.wait_ge(projected, 1)
                    turn = group + (group > QT * 2)
                    copy(attT[:, group % 4, :], bank[6 + turn % 2][:, 0:S]).then_inc(attT_done, 1)
            act.wait_ge(var_done, 2)
            nc.scalar.activation(std[:], mv[:, :, 1], ACT.Sqrt, bias=eps[:]).then_inc(std_done, 1)
            for t in range(TILES):
                act.wait_ge(xn2_turned, t + 1)
                if t >= 2:
                    act.wait_ge(logits_done, t - 1)
                copy(xn2T[t % 2].rearrange("p k t -> p (k t)"), bank[t][:, 0:KC * P]).then_inc(xn2T_done, 1)
            act.wait_ge(shifted, 1)
            nc.scalar.activation(rp, rp, ACT.Exp).then_inc(routed, 1)

            def step(s, late_part):
                a = s
                if a.exists():
                    act.wait_ge(gu_mm, a.e + 1)
                    if a.from_(2):
                        act.wait_ge(hid_done, a.e - 1)
                    nc.scalar.activation(sil[a.slot % 2], bank[3 + a.slot % 2][:, 0:I], ACT.Silu).then_inc(silu_done, 1)
                a = s.plus(-2)
                if a.exists():
                    act.wait_ge(y_mm, a.e + 1)
                    w = slot_weight[:, bass.ds(a.e, 1)]
                    if late_part and a.from_(EARLY):
                        if a.from_(EARLY + 1):
                            act.wait_ge(scattered, a.e - EARLY)
                        nc.scalar.activation(y_high[:], bank[2][:, 0:H], ACT.Copy, scale=w).then_inc(y_high_done, 1)
                    else:
                        if a.from_(Y_RING):
                            act.wait_ge(y_out[a.slot], a.i * 16)
                        nc.scalar.activation(y_sb[a.slot], bank[2][:, 0:H], ACT.Copy, scale=w).then_inc(y_done, 1)
                a = s.plus(-1)
                if a.exists():
                    act.wait_ge(hid_turned, a.e + 1)
                    if a.from_(2):
                        act.wait_ge(y_mm, a.e - 1)
                    copy(hT[a.slot % 2], bank[5][0:I, 0:P]).then_inc(hT_done, 1)

            pipeline(act, step)

        @block.vector
        def _(dve):
            v = nc.vector
            steps = [0]

            def then(ins):
                steps[0] += 1
                ins.then_inc(dve_step, 1)
                dve.wait_ge(dve_step, steps[0])

            dve.wait_ge(x_in, 16)
            for t in range(TILES):
                then(v.bn_stats(stats[:, t, :], x_sb[:, t, :]))
            for t in range(TILES):
                last = v.bn_aggr(mv[:, t, :], stats[:, t, :])
            last.then_inc(var_done, 1)
            dve.wait_ge(turned, 1)
            v.tensor_copy(wkT, bank[1][0:L, 0:H]).then_inc(wkvT_done, 1)
            v.tensor_copy(wvT, bank[1][0:L, H:2 * H]).then_inc(wkvT_done, 1)
            dve.wait_ge(std_done, 1)
            then(v.reciprocal(rstd[:], std[:]))
            for t in range(TILES):
                v.tensor_scalar(xn[:, t, :], x_sb[:, t, :], mv[:, t, 0:1], rstd[:, t:t + 1],
                                ALU.subtract, ALU.mult).then_inc(xn_done, 1)
            dve.wait_ge(turned, 3)
            v.tensor_scalar(wqT.rearrange("p k n -> p (k n)"), bank[0][:], -float(HD) ** -0.5, None,
                            ALU.mult).then_inc(wqT_done, 1)

            dve.wait_ge(heads_built, 3)
            dve.wait_ge(k_mm, 1)
            for h in range(NH // 2):
                v.tensor_scalar(kT[:, h, :], bank[4][:], head_rows[:, h:h + 1], None, ALU.mult).then_inc(k_dve, 1)
            dve.wait_ge(v_mm, 1)
            v.tensor_copy(v_sb[:, 0:QT, :, 0:HD],
                          bank[0][:].rearrange("p (t h d) -> p t h d", t=QT, d=HD)).then_inc(v_done, 1)
            dve.wait_ge(turned, 5)
            v.tensor_copy(xnT[:, 0, :], bank[2][:]).then_inc(xnT_done, 1)
            dve.wait_ge(q_mm, 1)
            v.tensor_copy(qT[:, 0, :], bank[6][:]).then_inc(q_done, 1)

            def mask_scores(n):
                dve.wait_ge(scored, n + 1)
                if n >= SCORES:
                    dve.wait_ge(probs_turned, n - SCORES + 1)
                for qt, cols in enumerate((slice(0, P), slice(P, 3 * P))):
                    v.tensor_tensor_reduce(score[n % SCORES][:, cols], bank[n % 4][:, cols], mask[:, cols], 1.0, BIG,
                                           ALU.add, ALU.min, rmin[:, n, qt:qt + 1]).then_inc(masked, 1)

            def residual(b):
                dve.wait_ge(projected, b + 1)
                for qt in range(QT):
                    t = QT * b + qt
                    v.scalar_tensor_tensor(out=x_sb[:, t, :], in0=bank[7][:, qt * H:qt * H + H],
                                           scalar=tgates[:, 0:1], in1=x_sb[:, t, :],
                                           op0=ALU.mult, op1=ALU.add).then_inc(x1_done, 1)
                for qt in range(QT):
                    t = QT * b + qt
                    dve.wait_ge(x1_done, t + 1)
                    last = v.bn_stats(stats[:, t, :], x_sb[:, t, :])
                then(last)
                for qt in range(QT):
                    t = QT * b + qt
                    last = v.bn_aggr(mv[:, t, :], stats[:, t, :])
                if b == B - 1:
                    last.then_inc(var_done, 1)

            dve.wait_ge(tanh_done, 1)
            dve.wait_ge(consts, n_consts[0])
            for i in range(HEADS + 3):
                if i < HEADS:
                    mask_scores(i)
                n = i - 1
                if 0 <= n < HEADS:
                    dve.wait_ge(exped, 2 * n + 2)
                    v.reciprocal(rrec[:, n, :], rsum[:, n, :]).then_inc(inverted, 1)
                n = i - 3
                if 0 <= n < HEADS and n % 2 == 1:
                    dve.wait_ge(probs_turned, n + 1)
                    if n >= 2:
                        dve.wait_ge(pv_done, n - 1)
                    v.tensor_copy(probT[1], bank[5][:, 0:3 * P]).then_inc(probT_dve, 1)
                if i == NH + 6:
                    residual(0)
            residual(1)

            dve.wait_ge(std_done, 2)
            then(v.reciprocal(rstd[:], std[:]))
            for t in range(TILES):
                v.tensor_scalar(xn[:, t, :], x_sb[:, t, :], mv[:, t, 0:1], rstd[:, t:t + 1],
                                ALU.subtract, ALU.mult).then_inc(xn2_done, 1)

            def over_experts(a):
                return a.unsqueeze(2).broadcast_to([P, TILES, E])

            dve.wait_ge(logits_done, TILES)
            logits = bank[6][:, 0:TILES * E].rearrange("p (t e) -> p t e", t=TILES)
            then(v.tensor_reduce(rstat[:, 0, :], logits, AX.X, ALU.max))
            v.tensor_tensor(rp, logits, over_experts(rstat[:, 0, :]), ALU.subtract).then_inc(shifted, 1)
            dve.wait_ge(routed, 1)
            then(v.tensor_reduce(rstat[:, 1, :], rp, AX.X, ALU.add))
            then(v.reciprocal(rstat[:, 1, :], rstat[:, 1, :]))
            then(v.tensor_tensor(rp, rp, over_experts(rstat[:, 1, :]), ALU.mult))
            for t in range(TILES):
                last = v.max(top[:, t, :], rp[:, t, :])
            then(last)
            for t in range(TILES):
                last = v.match_replace(rp2[:, t, :], top[:, t, :], rp[:, t, :], -1.0)
            then(last)
            v.tensor_scalar(rselb, rp2, 0.0, None, ALU.is_lt).then_inc(selected, 1)
            then(v.tensor_reduce(rstat[:, 2, :], top, AX.X, ALU.add))
            then(v.reciprocal(rstat[:, 2, :], rstat[:, 2, :]))
            then(v.tensor_scalar(rstat[:, 2, :], rstat[:, 2, :], tgates[:, 1:2], None, ALU.mult))
            then(v.tensor_tensor(rp, rp, over_experts(rstat[:, 2, :]), ALU.mult))
            then(v.tensor_copy(ids[:, :, :, 2], rp))
            then(v.tensor_tensor(rrest, rp, ids[:, :, :, 2], ALU.subtract))
            then(v.tensor_copy(ids[:, :, :, 3], rrest))
            v.tensor_tensor(ids[:, :, :, 4], rrest, ids[:, :, :, 3], ALU.subtract)
            dve.wait_ge(counted, 1)
            before = bank[7][:, 0:TILES * E].rearrange("p (t e) -> p t e", t=TILES)
            then(v.scalar_tensor_tensor(out=place1[:], in0=before, scalar=1.0, in1=rselb, op0=ALU.add, op1=ALU.mult))

            def find_rows():
                early = before[:, :, 0:EARLY]
                v.scalar_tensor_tensor(out=valid, in0=early, scalar=float(CAP), in1=rselb[:, :, 0:EARLY],
                                       op0=ALU.is_lt, op1=ALU.mult)
                then(v.scalar_tensor_tensor(out=far, in0=early, scalar=-1.0,
                                            in1=expert_far[:].unsqueeze(1).broadcast_to([P, TILES, EARLY]),
                                            op0=ALU.mult, op1=ALU.add))
                then(v.tensor_tensor(far, far, valid, ALU.mult))
                for t in range(TILES):
                    last = v.max(far8[:, t, :], far[:, t, :])
                then(last)
                v.tensor_scalar(row8[:], far8.rearrange("p t k -> p (t k)"), -1.0, float(FAR),
                                ALU.mult, ALU.add).then_inc(rows_ready, 1)

            def add_rows(c):
                dve.wait_ge(c_in[c.slot], c.i * 16 + 16)
                if c.from_(TILES):
                    dve.wait_ge(added, c.e - (TILES - 1))
                v.tensor_tensor(x_sb[:, c.slot, :], x_sb[:, c.slot, :],
                                c_sb[:, bass.ds(c.e, 1), :].rearrange("p a n -> p (a n)"), ALU.add).then_inc(added, 1)

            def step(s, late_part):
                a = s.plus(LOOKAHEAD)
                if a.exists():
                    if a.from_(2):
                        dve.wait_ge(slots_mm, a.e - 1)
                    for t in range(TILES):
                        last = v.tensor_scalar(onehot[a.slot % 2][:, t, :], slot1[:],
                                               place1[:].rearrange("p t e -> p (t e)")[:, bass.ds(a.e + t * E, 1)],
                                               None, ALU.is_equal)
                    last.then_inc(onehot_done, 1)
                a = s.plus(LOOKAHEAD - 1)
                if a.exists():
                    dve.wait_ge(slots_mm, a.e + 1)
                    v.tensor_scalar(slot_token[:, bass.ds(a.e, 1)], bank[0][:, 0:1], float(NO_TOKEN),
                                    bank[0][:, 1:2], ALU.add, ALU.add)
                    v.tensor_reduce(slot_weight[:, bass.ds(a.e, 1)], bank[0][:, 2:IDS], AX.X,
                                    ALU.add).then_inc(slots_done, 1)
                if s.static and s.e == -2:
                    find_rows()
                a = s.plus(1)
                if a.exists():
                    dve.wait_ge(xe_turned, a.e + 1)
                    if a.from_(2):
                        dve.wait_ge(gu_mm, a.e - 1)
                    v.tensor_copy(xeT[a.slot % 2].rearrange("p k t -> p (k t)"),
                                  bank[1][:, 0:KC * P]).then_inc(xeT_done, 1)
                a = s
                if a.exists():
                    dve.wait_ge(silu_done, a.e + 1)
                    if a.from_(2):
                        dve.wait_ge(hid_turned, a.e - 1)
                    v.tensor_tensor(hid[a.slot % 2], sil[a.slot % 2], bank[3 + a.slot % 2][:, I:2 * I],
                                    ALU.mult).then_inc(hid_done, 1)
                a = s.plus(-2)
                if late_part and a.exists() and a.from_(EARLY):
                    if a.from_(EARLY + 1):
                        dve.wait_ge(scattered, a.e - EARLY)
                    v.tensor_scalar(scatter[:], tokens[:], slot_token[:, bass.ds(a.e, 1)], None,
                                    ALU.is_equal).then_inc(scatter_done, 1)
                    dve.wait_ge(y_high_done, a.e - (EARLY - 1))
                    v.scalar_tensor_tensor(out=y_low[:], in0=bank[2][:, 0:H], scalar=slot_weight[:, bass.ds(a.e, 1)],
                                           in1=y_high[:].bitcast(F32), op0=ALU.mult,
                                           op1=ALU.subtract).then_inc(y_low_done, 1)
                if s.static and s.e < ADDS_FROM:
                    return
                if late_part:
                    if s.static and s.e >= TWO_ADDS_FROM:
                        c = TWO_ADDS_FROM - ADDS_FROM + 2 * (s.e - TWO_ADDS_FROM)
                        for n in (c, c + 1):
                            if n < ROWS:
                                add_rows(Expert(0, n))
                    else:
                        add_rows(s.plus(-ADDS_FROM))

            pipeline(dve, step)
            dve.wait_ge(scattered, E - EARLY)
            dve.wait_ge(added, ROWS)
            for t in range(TILES):
                v.tensor_tensor(xn[:, t, :], bank[6 + t // 2][:, (t % 2) * H:(t % 2) * H + H], x_sb[:, t, :],
                                ALU.add).then_inc(out_done, 1)


_INS = ['x', 'ctx_512', 'g_xattn', 'g_ffn', 'L0_xattn_Wq', 'L0_xattn_Wkv_expand', 'L0_xattn_Wout',
        'L0_ffn_router_weight', 'L0_ffn_gate_up_proj', 'L0_ffn_down_proj']
_OUTS = [((B, S, H), 'float32')]


def kernel(**inputs):
    import numpy as _np
    import concourse.bacc as _bacc
    from concourse import mybir as _mybir
    from concourse.bass_utils import run_bass_kernel_spmd as _run

    nc = _bacc.Bacc("TRN2", target_bir_lowering=False, num_devices=1)
    arrays, args = {}, []
    for name in _INS:
        a = _np.ascontiguousarray(inputs[name])
        arrays[f"in_{name}_dram"] = a
        args.append(nc.dram_tensor(f"in_{name}_dram", a.shape, _mybir.dt.from_np(a.dtype), kind="ExternalInput").ap())
    for i, (shape, dtype) in enumerate(_OUTS):
        dt = _mybir.dt.from_np(_np.dtype(dtype))
        args.append(nc.dram_tensor(f"out_{i}_dram", shape, dt, kind="ExternalOutput").ap())
    flamingo_moe(nc, *args)
    r = _run(nc, [arrays], core_ids=[0])
    got = tuple(r.results[0][f"out_{i}_dram"] for i in range(len(_OUTS)))
    return got[0]
```
